# Optimizing a Trainium2 kernel written in Bass

```python
import numpy as np
import jax
import jax.numpy as jnp

def _softmax(x, axis=-1):
    return jax.nn.softmax(x, axis=axis)

def _gelu(x):
    return jax.nn.gelu(x, approximate=True)

def _silu(x):
    return jax.nn.silu(x)

def _sigmoid(x):
    return jax.nn.sigmoid(x)

def _layernorm(x, axis=-1, eps=1e-05):
    m = jnp.mean(x, axis=axis, keepdims=True)
    v = jnp.var(x, axis=axis, keepdims=True)
    return (x - m) / jnp.sqrt(v + eps)

def _scatter_add(tgt, idx, src, axis=0):
    return tgt.at[idx].add(src)

def _segment_sum(src, seg, n):
    return jax.ops.segment_sum(src, seg, n)
kernel_name = 'mk_pixart_resid_d2_seqx_r4_0a0f34'

def setup_inputs(seed: int=0):
    np.random.seed(seed)
    _w = jnp.asarray

    def _rec_inputs():
        import jax
        import jax.numpy as jnp
        _rk = jax.random.key(seed)
        x = -0.0002928 + 1 * jax.random.normal(jax.random.fold_in(_rk, 1), (8, 256, 256), jnp.float32)
        _lenS = 256 - jax.random.randint(jax.random.fold_in(_rk, 7), (8,), 0, max(1, 256 // 4) + 1, jnp.int32)
        _lenS2 = 120 - jax.random.randint(jax.random.fold_in(_rk, 8), (8,), 0, max(1, 120 // 4) + 1, jnp.int32)
        _ctx_1024P = jax.random.normal(jax.random.fold_in(_rk, 11), (8, 16, 256), jnp.float32)
        _ctx_1024c = jax.random.dirichlet(jax.random.fold_in(_rk, 511), 0.3 * jnp.ones((16,), jnp.float32), (8, 120))
        _ctx_1024t = jnp.einsum('bsk,bkd->bsd', _ctx_1024c, _ctx_1024P)
        _ctx_1024t = _ctx_1024t * jax.lax.rsqrt(jnp.mean(jnp.square(_ctx_1024t)) + 1e-12) * 0.953939
        ctx_1024 = -1.39393e-06 + 0.999914 * (_ctx_1024t + 0.3 * jax.random.normal(jax.random.fold_in(_rk, 611), (8, 120, 256), jnp.float32))
        condB_tau = jax.random.uniform(jax.random.fold_in(_rk, 12), (8,), jnp.float32, 0.0, 1.23395)
        fside_BxS2_0 = -0.00205293 + 0.99739 * jax.random.normal(jax.random.fold_in(_rk, 13), (8, 120), jnp.float32)
        return (x, ctx_1024, condB_tau, fside_BxS2_0)
    x, ctx_1024, condB_tau, fside_BxS2_0 = _rec_inputs()

    def _L0_xcond_setup():
        import jax, jax.numpy as jnp
        import numpy as np
        B, S, D, H = (2, 512, 256, 16)
        DK = D // H

        def _split_heads(x):
            b, s, _ = x.shape
            return x.reshape(b, s, H, DK).transpose(0, 2, 1, 3)
        key = jax.random.key(seed)
        ks = jax.random.split(key, 14)
        inp = {'query': jax.random.normal(ks[0], (B, S, D), jnp.float32), 'key': jax.random.normal(ks[1], (B, S, D), jnp.float32), 'value': jax.random.normal(ks[2], (B, S, D), jnp.float32), 'tau': jax.random.uniform(ks[3], (B, 1), jnp.float32, 0.5, 1.5), 'delta': jax.random.normal(ks[4], (B, S), jnp.float32)}
        sc = 1.0 / np.sqrt(D)
        for i, name in enumerate(['q', 'k', 'v', 'o']):
            inp[f'W{name}'] = jax.random.normal(ks[5 + 2 * i], (D, D), jnp.float32) * sc
            inp[f'b{name}'] = jax.random.normal(ks[6 + 2 * i], (D,), jnp.float32) * 0.01
        return inp
    _L0_xcond_all = _L0_xcond_setup()
    _L0_xcond_in = {k: v for k, v in _L0_xcond_all.items() if k in ('Wq', 'bq', 'Wk', 'bk', 'Wv', 'bv', 'Wo', 'bo')}
    del _L0_xcond_all

    def _L0_ffn_setup():
        import jax, jax.numpy as jnp
        import numpy as np
        B, S, H, NH, E, F = (4, 256, 256, 16, 8, 1024)
        D = H // NH
        EPS = 1e-05

        def _layernorm(x, g, b):
            mu = jnp.mean(x, axis=-1, keepdims=True)
            var = jnp.var(x, axis=-1, keepdims=True)
            return (x - mu) * jax.lax.rsqrt(var + EPS) * g + b
        key = jax.random.key(seed)
        ks = jax.random.split(key, 16)
        s = 0.02
        return {'x': jax.random.normal(ks[0], (B, S, H), jnp.float32), 'ln1_g': jnp.ones((H,), jnp.float32), 'ln1_b': jnp.zeros((H,), jnp.float32), 'ln2_g': jnp.ones((H,), jnp.float32), 'ln2_b': jnp.zeros((H,), jnp.float32), 'wq': jax.random.normal(ks[1], (H, H), jnp.float32) * s, 'bq': jnp.zeros((H,), jnp.float32), 'wk': jax.random.normal(ks[2], (H, H), jnp.float32) * s, 'bk': jnp.zeros((H,), jnp.float32), 'wv': jax.random.normal(ks[3], (H, H), jnp.float32) * s, 'bv': jnp.zeros((H,), jnp.float32), 'wo': jax.random.normal(ks[4], (H, H), jnp.float32) * s, 'bo': jnp.zeros((H,), jnp.float32), 'gate_w': jax.random.normal(ks[5], (H, E), jnp.float32) * s, 'gate_b': jnp.zeros((E,), jnp.float32), 'w1': jax.random.normal(ks[6], (E, H, F), jnp.float32) * s, 'b1': jnp.zeros((E, F), jnp.float32), 'w2': jax.random.normal(ks[7], (E, F, H), jnp.float32) * s, 'b2': jnp.zeros((E, H), jnp.float32)}
    _L0_ffn_all = _L0_ffn_setup()
    _L0_ffn_in = {k: v for k, v in _L0_ffn_all.items() if k in ('ln1_g', 'ln1_b', 'ln2_g', 'ln2_b', 'wq', 'bq', 'wk', 'bk', 'wv', 'bv', 'wo', 'bo', 'gate_w', 'gate_b', 'w1', 'b1', 'w2', 'b2')}
    del _L0_ffn_all

    def _L1_xcond_setup():
        import jax, jax.numpy as jnp
        import numpy as np
        D_MODEL = 256
        N_HEADS = 16
        key = jax.random.key(seed)
        ks = jax.random.split(key, 16)
        B, L, S, D = (4, 512, 512, D_MODEL)
        inp = {'q': jax.random.normal(ks[0], (B, L, D), jnp.float32), 'k': jax.random.normal(ks[1], (B, S, D), jnp.float32), 'v': jax.random.normal(ks[2], (B, S, D), jnp.float32), 'tau': jax.random.uniform(ks[3], (B, 1), jnp.float32, 0.5, 1.5), 'delta': jax.random.normal(ks[4], (B, S), jnp.float32)}
        s = 1.0 / np.sqrt(D)
        inp['Wq'] = jax.random.normal(ks[5], (D, D), jnp.float32) * s
        inp['bq'] = jnp.zeros((D,), jnp.float32)
        inp['Wk'] = jax.random.normal(ks[6], (D, D), jnp.float32) * s
        inp['bk'] = jnp.zeros((D,), jnp.float32)
        inp['Wv'] = jax.random.normal(ks[7], (D, D), jnp.float32) * s
        inp['bv'] = jnp.zeros((D,), jnp.float32)
        inp['Wo'] = jax.random.normal(ks[8], (D, D), jnp.float32) * s
        inp['bo'] = jnp.zeros((D,), jnp.float32)
        return inp
    _L1_xcond_all = _L1_xcond_setup()
    _L1_xcond_in = {k: v for k, v in _L1_xcond_all.items() if k in ('Wq', 'bq', 'Wk', 'bk', 'Wv', 'bv', 'Wo', 'bo')}
    del _L1_xcond_all

    def _L1_ffn_setup():
        import jax, jax.numpy as jnp
        import numpy as np
        DM, NEXPERTS, SETS, ESIZE = (256, 32, 4, 32)
        B, S = (2, 2048)
        key = jax.random.key(seed)
        ks = jax.random.split(key, 7)
        sc = 0.02
        return {'x': jax.random.normal(ks[0], (B, S, DM), jnp.float32), 'Wc': jax.random.normal(ks[1], (DM, NEXPERTS, SETS), jnp.float32) * sc, 'bc': jax.random.normal(ks[2], (NEXPERTS, SETS), jnp.float32) * sc, 'W1': jax.random.normal(ks[3], (NEXPERTS, SETS, DM, ESIZE), jnp.float32) * sc, 'b1': jax.random.normal(ks[4], (NEXPERTS, SETS, ESIZE), jnp.float32) * sc, 'W2': jax.random.normal(ks[5], (NEXPERTS, SETS, DM, ESIZE), jnp.float32) * sc, 'b2': jax.random.normal(ks[6], (NEXPERTS, SETS, DM), jnp.float32) * sc}
    _L1_ffn_all = _L1_ffn_setup()
    _L1_ffn_in = {k: v for k, v in _L1_ffn_all.items() if k in ('Wc', 'bc', 'W1', 'b1', 'W2', 'b2')}
    del _L1_ffn_all
    return {'x': x, 'ctx_1024': ctx_1024, 'condB_tau': condB_tau, 'fside_BxS2_0': fside_BxS2_0, 'L0_xcond_Wq': _L0_xcond_in['Wq'], 'L0_xcond_bq': _L0_xcond_in['bq'], 'L0_xcond_Wk': _L0_xcond_in['Wk'], 'L0_xcond_bk': _L0_xcond_in['bk'], 'L0_xcond_Wv': _L0_xcond_in['Wv'], 'L0_xcond_bv': _L0_xcond_in['bv'], 'L0_xcond_Wo': _L0_xcond_in['Wo'], 'L0_xcond_bo': _L0_xcond_in['bo'], 'L0_ffn_ln1_g': _L0_ffn_in['ln1_g'], 'L0_ffn_ln1_b': _L0_ffn_in['ln1_b'], 'L0_ffn_ln2_g': _L0_ffn_in['ln2_g'], 'L0_ffn_ln2_b': _L0_ffn_in['ln2_b'], 'L0_ffn_wq': _L0_ffn_in['wq'], 'L0_ffn_bq': _L0_ffn_in['bq'], 'L0_ffn_wk': _L0_ffn_in['wk'], 'L0_ffn_bk': _L0_ffn_in['bk'], 'L0_ffn_wv': _L0_ffn_in['wv'], 'L0_ffn_bv': _L0_ffn_in['bv'], 'L0_ffn_wo': _L0_ffn_in['wo'], 'L0_ffn_bo': _L0_ffn_in['bo'], 'L0_ffn_gate_w': _L0_ffn_in['gate_w'], 'L0_ffn_gate_b': _L0_ffn_in['gate_b'], 'L0_ffn_w1': _L0_ffn_in['w1'], 'L0_ffn_b1': _L0_ffn_in['b1'], 'L0_ffn_w2': _L0_ffn_in['w2'], 'L0_ffn_b2': _L0_ffn_in['b2'], 'L1_xcond_Wq': _L1_xcond_in['Wq'], 'L1_xcond_bq': _L1_xcond_in['bq'], 'L1_xcond_Wk': _L1_xcond_in['Wk'], 'L1_xcond_bk': _L1_xcond_in['bk'], 'L1_xcond_Wv': _L1_xcond_in['Wv'], 'L1_xcond_bv': _L1_xcond_in['bv'], 'L1_xcond_Wo': _L1_xcond_in['Wo'], 'L1_xcond_bo': _L1_xcond_in['bo'], 'L1_ffn_Wc': _L1_ffn_in['Wc'], 'L1_ffn_bc': _L1_ffn_in['bc'], 'L1_ffn_W1': _L1_ffn_in['W1'], 'L1_ffn_b1': _L1_ffn_in['b1'], 'L1_ffn_W2': _L1_ffn_in['W2'], 'L1_ffn_b2': _L1_ffn_in['b2']}

def reference(x, ctx_1024, condB_tau, fside_BxS2_0, L0_xcond_Wq, L0_xcond_bq, L0_xcond_Wk, L0_xcond_bk, L0_xcond_Wv, L0_xcond_bv, L0_xcond_Wo, L0_xcond_bo, L0_ffn_ln1_g, L0_ffn_ln1_b, L0_ffn_ln2_g, L0_ffn_ln2_b, L0_ffn_wq, L0_ffn_bq, L0_ffn_wk, L0_ffn_bk, L0_ffn_wv, L0_ffn_bv, L0_ffn_wo, L0_ffn_bo, L0_ffn_gate_w, L0_ffn_gate_b, L0_ffn_w1, L0_ffn_b1, L0_ffn_w2, L0_ffn_b2, L1_xcond_Wq, L1_xcond_bq, L1_xcond_Wk, L1_xcond_bk, L1_xcond_Wv, L1_xcond_bv, L1_xcond_Wo, L1_xcond_bo, L1_ffn_Wc, L1_ffn_bc, L1_ffn_W1, L1_ffn_b1, L1_ffn_W2, L1_ffn_b2):
    import jax
    import jax.numpy as jnp

    def _L0_xcond_ref(query, key, value, tau, delta, Wq, bq, Wk, bk, Wv, bv, Wo, bo):
        import jax, jax.numpy as jnp
        import numpy as np
        B, S, D, H = (2, 512, 256, 16)
        DK = D // H

        def _split_heads(x):
            b, s, _ = x.shape
            return x.reshape(b, s, H, DK).transpose(0, 2, 1, 3)
        q = _split_heads(query @ Wq.T + bq)
        k = _split_heads(key @ Wk.T + bk)
        v = _split_heads(value @ Wv.T + bv)
        scores = jnp.einsum('bhqd,bhkd->bhqk', q, k)
        scores = scores * tau[:, :, None, None] + delta[:, None, None, :]
        scores = scores / jnp.sqrt(jnp.asarray(DK, scores.dtype))
        p_attn = jax.nn.softmax(scores, axis=-1)
        x = jnp.einsum('bhqk,bhkd->bhqd', p_attn, v)
        x = x.transpose(0, 2, 1, 3).reshape(query.shape[0], -1, H * DK)
        return x @ Wo.T + bo

    def _L0_ffn_ref(x, ln1_g, ln1_b, ln2_g, ln2_b, wq, bq, wk, bk, wv, bv, wo, bo, gate_w, gate_b, w1, b1, w2, b2):
        import jax, jax.numpy as jnp
        import numpy as np
        B, S, H, NH, E, F = (4, 256, 256, 16, 8, 1024)
        D = H // NH
        EPS = 1e-05

        def _layernorm(x, g, b):
            mu = jnp.mean(x, axis=-1, keepdims=True)
            var = jnp.var(x, axis=-1, keepdims=True)
            return (x - mu) * jax.lax.rsqrt(var + EPS) * g + b
        b, s, h = x.shape
        hn = _layernorm(x, ln1_g, ln1_b)
        q = (hn @ wq + bq).reshape(b, s, NH, D).transpose(0, 2, 1, 3)
        k = (hn @ wk + bk).reshape(b, s, NH, D).transpose(0, 2, 1, 3)
        v = (hn @ wv + bv).reshape(b, s, NH, D).transpose(0, 2, 1, 3)
        scores = jnp.einsum('bhqd,bhkd->bhqk', q, k) / jnp.sqrt(jnp.float32(D))
        attn = jax.nn.softmax(scores, axis=-1)
        o = jnp.einsum('bhqk,bhkd->bhqd', attn, v)
        o = o.transpose(0, 2, 1, 3).reshape(b, s, h)
        x = x + (o @ wo + bo)
        hn2 = _layernorm(x, ln2_g, ln2_b).reshape(-1, h)
        logits = hn2 @ gate_w + gate_b
        idx = jnp.argmax(logits, axis=-1)
        mid = jax.nn.relu(jnp.einsum('th,ehf->etf', hn2, w1) + b1[:, None, :])
        y = jnp.einsum('etf,efh->eth', mid, w2) + b2[:, None, :]
        moe = y[idx, jnp.arange(hn2.shape[0])]
        return x + moe.reshape(b, s, h)

    def _L1_xcond_ref(q, k, v, tau, delta, Wq, bq, Wk, bk, Wv, bv, Wo, bo):
        import jax, jax.numpy as jnp
        import numpy as np
        D_MODEL = 256
        N_HEADS = 16
        B, L, D = q.shape
        S = k.shape[1]
        H = N_HEADS
        E = D // H
        qh = (q @ Wq.T + bq).reshape(B, L, H, E)
        kh = (k @ Wk.T + bk).reshape(B, S, H, E)
        vh = (v @ Wv.T + bv).reshape(B, S, H, E)
        scale = 1.0 / np.sqrt(E).astype(np.float32)
        scores = jnp.einsum('blhe,bshe->bhls', qh, kh)
        scores = scores * tau[:, None, None, :] + delta[:, None, None, :]
        a = jax.nn.softmax(scale * scores, axis=-1)
        out = jnp.einsum('bhls,bshd->blhd', a, vh).reshape(B, L, D)
        return out @ Wo.T + bo

    def _L1_ffn_ref(x, Wc, bc, W1, b1, W2, b2):
        import jax, jax.numpy as jnp
        import numpy as np
        DM, NEXPERTS, SETS, ESIZE = (256, 32, 4, 32)
        B, S = (2, 2048)
        b, s, d = x.shape
        g = Wc.shape[1]
        grouped = x.reshape(b, s // g, g, d)
        logits = jnp.einsum('bntd,des->bntes', grouped, Wc) + bc
        tie = jnp.linspace(0.0, 1e-06, g, dtype=x.dtype).reshape(-1, 1, 1)
        logits = logits + tie
        perm = (logits == jnp.max(logits, axis=-3, keepdims=True)).astype(x.dtype)
        permuted = jnp.einsum('bntd,bntes->bnesd', grouped, perm)
        inner = jax.nn.relu(jnp.einsum('bnesd,esdf->bnesf', permuted, W1) + b1)
        result_permuted = jnp.einsum('bnesf,esdf->bnesd', inner, W2) + b2
        result = jnp.einsum('bnesd,bntes->bntd', result_permuted, perm)
        return result.reshape(b, s, d)
    x = x + _L0_xcond_ref(_layernorm(x, axis=-1), ctx_1024, ctx_1024, condB_tau[:, None], fside_BxS2_0, L0_xcond_Wq, L0_xcond_bq, L0_xcond_Wk, L0_xcond_bk, L0_xcond_Wv, L0_xcond_bv, L0_xcond_Wo, L0_xcond_bo)
    x = x + _L0_ffn_ref(_layernorm(x, axis=-1), L0_ffn_ln1_g, L0_ffn_ln1_b, L0_ffn_ln2_g, L0_ffn_ln2_b, L0_ffn_wq, L0_ffn_bq, L0_ffn_wk, L0_ffn_bk, L0_ffn_wv, L0_ffn_bv, L0_ffn_wo, L0_ffn_bo, L0_ffn_gate_w, L0_ffn_gate_b, L0_ffn_w1, L0_ffn_b1, L0_ffn_w2, L0_ffn_b2)
    x = x + _L1_xcond_ref(_layernorm(x, axis=-1), ctx_1024, ctx_1024, condB_tau[:, None], fside_BxS2_0, L1_xcond_Wq, L1_xcond_bq, L1_xcond_Wk, L1_xcond_bk, L1_xcond_Wv, L1_xcond_bv, L1_xcond_Wo, L1_xcond_bo)
    x = x + _L1_ffn_ref(_layernorm(x, axis=-1), L1_ffn_Wc, L1_ffn_bc, L1_ffn_W1, L1_ffn_b1, L1_ffn_W2, L1_ffn_b2)
    return x

_drawn_inputs = setup_inputs


def setup_inputs(seed=0):
    import zlib

    import numpy as np

    out = dict(_drawn_inputs(seed))
    spreads = {'L0_ffn_ln1_g': (1.0, 0.6),
     'L0_ffn_ln1_b': (0.0, 0.799),
     'L0_ffn_ln2_g': (1.0, 0.2),
     'L0_ffn_ln2_b': (0.0, 0.1),
     'L0_ffn_bq': (0.0, 0.8),
     'L0_ffn_bk': (0.0, 2.0),
     'L0_ffn_bv': (0.0, 0.428),
     'L0_ffn_bo': (0.0, 0.1),
     'L0_ffn_gate_b': (0.0, 0.1),
     'L0_ffn_b1': (0.0, 0.381),
     'L0_ffn_b2': (0.0, 0.1),
     'L1_xcond_bq': (0.0, 0.8),
     'L1_xcond_bk': (0.0, 2.0),
     'L1_xcond_bv': (0.0, 0.1),
     'L1_xcond_bo': (0.0, 0.1)}
    factors = {'L0_xcond_bq': 27.417,
     'L0_xcond_bk': 64.0,
     'L0_xcond_bv': 4.54,
     'L0_xcond_bo': 4.993,
     'L0_ffn_wq': 8.0,
     'L0_ffn_wk': 8.0,
     'L1_ffn_W1': 2.958,
     'L1_ffn_b1': 40.212,
     'L1_ffn_b2': 3.136}
    for name, (base, spread) in spreads.items():
        noise = np.random.default_rng([zlib.crc32(name.encode()), seed]).standard_normal(out[name].shape)
        drawn = base * np.exp(spread * noise) if base else spread * noise
        out[name] = jnp.asarray(drawn.astype(out[name].dtype))
    for name, factor in factors.items():
        out[name] = (out[name] * factor).astype(out[name].dtype)
    return out
```

```python
from contextlib import ExitStack

import concourse.bass as bass
from concourse import mybir
from concourse.alu_op_type import AluOpType as ALU

F32 = mybir.dt.float32
BF = mybir.dt.bfloat16
I32 = mybir.dt.int32
U32 = mybir.dt.uint32
ACT = mybir.ActivationFunctionType
AX = mybir.AxisListType

NT = 16
NB = 8
CK = 120
NTILE = 23
EPS = 1e-5
QP = (0, 0, 0, 1, 1, 2)
KP = (0, 1, 2, 0, 1, 0)


class Queue:

    def __init__(self, sem, chained=False):
        self.sem, self.n, self.items, self.chained = sem, 0, [], chained

    def put(self, fn, waits=(), signal=True):
        token = None
        if self.chained and self.n:
            waits = (*waits, (self.sem, self.n))
        if signal:
            self.n += 1
            token = (self.sem, self.n)
        self.items.append((tuple(w for w in waits if w is not None), fn, self.sem if signal else None))
        return token

    def dma(self, fn, sem, waits=()):
        self.items.append((tuple(w for w in waits if w is not None), fn, (sem,)))


class Dmas:

    def __init__(self, sems):
        self.sems, self.count, self.at = sems, [0] * len(sems), -1

    def group(self, queue, items, waits=()):
        self.at = (self.at + 1) % len(self.sems)
        i = self.at
        before = (self.sems[i], self.count[i]) if self.count[i] else None
        for fn in items:
            queue.dma(fn, self.sems[i], (*waits, before))
            self.count[i] += 16
        return (self.sems[i], self.count[i])


class Ring:

    def __init__(self, bufs):
        self.bufs, self.free, self.at = bufs, [() for _ in bufs], -1

    def take(self):
        self.at = (self.at + 1) % len(self.bufs)
        return self.at, self.bufs[self.at], self.free[self.at]


def program(nc, D, out, stage):
    with ExitStack() as ctx:
        build(nc, D, out, stage, ctx)


def build(nc, D, out, stage, ctx):
    zb = nc.dram_tensor("zb", (NTILE * 128, 256), F32, kind="Internal").ap()
    yb = nc.dram_tensor("yb", (NTILE * 128, 256), F32, kind="Internal").ap()
    base = [nc.sbuf_base + (-nc.sbuf_base) % 64]

    def at(name, shape, dt, off):
        return nc.alloc_sbuf_tensor_at(name, shape, dt, offset=off)

    def size(shape, dt):
        n = 2 if dt == BF else 4
        for s in shape[1:]:
            n *= s
        return (n + 63) // 64 * 64

    class Area:
        def __init__(self, start):
            self.p, self.top = start, start

        def new(self, name, shape, dt=F32):
            t = at(name, shape, dt, self.p)
            self.p += size(shape, dt)
            assert self.p <= nc.sbuf_usable_end, (name, self.p, nc.sbuf_usable_end)
            return t

    def sem(name):
        return ctx.enter_context(nc.semaphore(name))

    pe, act, dve, pool, sp = (Queue(sem(f"s_{n}"), n == "pool") for n in ("pe", "act", "dve", "pool", "sp"))
    dq = Dmas([sem(f"d_q{i}") for i in range(8)])
    dm = Dmas([sem(f"d_m{i}") for i in range(4)])
    do = Dmas([sem(f"d_o{i}") for i in range(4)])
    dw = Dmas([sem(f"d_w{i}") for i in range(16)])
    dz = Dmas([sem(f"d_z{i}") for i in range(3)])
    dy = Dmas([sem(f"d_y{i}") for i in range(3)])
    ds = Dmas([sem("d_s")])
    dg = Dmas([sem(f"d_g{i}") for i in range(16)])
    dx = Dmas([sem(f"d_x{i}") for i in range(4)])

    g0 = Area(base[0])
    x = g0.new("x", [128, NT, 256])
    y = g0.new("y", [128, NT, 256])
    idf = g0.new("idf", [128, 128])
    idb = g0.new("idb", [128, 128], BF)
    vec = g0.new("vec", [128, 160])
    mhalf = g0.new("mhalf", [128, 16])
    st = g0.new("st", [128, 8, 6])
    mv = g0.new("mv", [128, 8, 2])
    ve = g0.new("ve", [128, 8])
    rs = g0.new("rs", [128, 8])
    oh = g0.new("oh", [128, NT, 8])
    nxt = g0.p

    PS = [nc.alloc_psum_tensor(f"PS{i}", [128, 1024], F32) for i in range(2)]
    U = nc.alloc_psum_tensor("U", [128, 512], F32)
    MB = [nc.alloc_psum_tensor(f"MB{i}", [128, 512], F32) for i in range(3)]

    V_BQ, V_BK = (0, 4, 8), (2, 6, 10)
    V_G1, V_B1, V_G2, V_B2 = 12, 14, 16, 18
    V_TAU, V_BC, V_BM1, V_BF1, V_GB = 20, 28, 29, 61, 125

    def vcol(i):
        return vec[:, i:i + 1]

    t_vec = dw.group(sp, [lambda e: e.dma_start(vec[:, 0:133], D["vec"])])
    t_idf = dw.group(sp, [lambda e: e.dma_start(idf[:, :], D["idf"])])
    xv = D["x"].rearrange("(t p) d -> p t d", p=128)
    t_x = [dw.group(act, [lambda e, i=i: e.dma_start(x[:, 4 * i:4 * i + 4, :], xv[:, 4 * i:4 * i + 4, :])])
           for i in range(4)]
    t_idb = pool.put(lambda e: e.tensor_copy(idb[:, :], idf[:, :]), [t_idf])
    t_mh = pool.put(lambda e: e.memset(mhalf[:, :], -0.5))
    x_ready = [t_x[t // 4] for t in range(NT)]
    st_free = [None]

    def norm(srcs, dsts, waits, dst_waits=()):
        n = len(srcs)
        first = [*waits, st_free[0], t_mh]
        for i, s in enumerate(srcs):
            t = dve.put(lambda e, i=i, s=s: e.bn_stats(st[:, i, :], s), first)
        for i in range(n):
            t = dve.put(lambda e, i=i: e.bn_aggr(mv[:, i, :], st[:, i, :]), [t])
        t = pool.put(lambda e: e.tensor_scalar(ve[:, 0:n], mv[:, 0:n, 1], EPS, None, ALU.add), [t])
        t = pool.put(lambda e: e.tensor_tensor(rs[:, 0:n], ve[:, 0:n], mhalf[:, 0:n], ALU.pow), [t])
        for i in range(n):
            t = pool.put(lambda e, i=i: e.tensor_scalar(dsts[i], srcs[i], mv[:, i, 0:1], rs[:, i:i + 1],
                                                        ALU.subtract, ALU.mult), [t, *dst_waits])
        st_free[0] = t
        return t

    M = Ring(MB)
    S = Ring(PS)
    ufree = [()]

    def attention(layer, area):
        cross = layer != 1
        NK = CK if cross else 128
        KT = 1 if cross else 2
        K1 = 99 if cross else 96
        K2 = K1 + 2
        W = area.new(f"W{layer}", [128, 2560])
        t_W = dw.group(sp, [lambda e: e.dma_start(W[:, :], D[f"W{layer}"])])
        wq = W[:, 0:512].rearrange("p (k n) -> p k n", k=2)
        wk = W[:, 512:1024].rearrange("p (k n) -> p k n", k=2)
        wv = W[:, 1024:1536].rearrange("p (k n) -> p k n", k=2)
        wo = W[:, 1536:2048].rearrange("p (k n) -> p k n", k=2)
        bv, bo = W[:, 2048:2304], W[:, 2304:2560]

        Qs = [area.new(f"Qs{layer}_{i}", [128, 16, 512], BF) for i in range(3)]
        if cross:
            Ks = [area.new(f"Ks{layer}", [128, 16, NB * CK], BF)]
            Va = [area.new(f"Va{layer}", [128, NB, 16, 32])]
        else:
            Ks = [area.new(f"Ks{layer}_{i}", [128, 16, 512], BF) for i in range(3)]
            Va = [area.new(f"Va{layer}_{i}", [128, 4, 16, 32]) for i in range(3)]
        P = Ring([area.new(f"P{layer}_{i}", [128, 1024]) for i in range(2)])
        Ub = Ring([area.new(f"Ub{layer}_{i}", [128, 512]) for i in range(1)])
        OL = Ring([area.new(f"OL{layer}_{i}", [128, 2, 2, 256]) for i in range(1)])
        z = area.new(f"z{layer}", [128, 4, 256])
        zT = area.new(f"zT{layer}", [128, 2, 512])
        tq = area.new(f"tq{layer}", [128, 512])
        rq = area.new(f"rq{layer}", [128, 512])
        SP3 = Ring([area.new(f"sp{layer}_{i}", [128, 3, 512], BF) for i in range(2)])
        nm = area.new(f"nm{layer}", [128, 16])
        Mh = Ring([area.new(f"Mh{layer}_{i}", [128, 32], BF) for i in range(2)])
        mT = Ring([area.new(f"mT{layer}_{i}", [32, 256], BF) for i in range(2)])
        if cross:
            zone = area.p
            ctx = area.new(f"ctx{layer}", [128, 2, NB * CK])
            t_ctx = dw.group(sp, [lambda e: e.dma_start(ctx[:, :, :], D["ctx"])])
            dr = area.new(f"dr{layer}", [8, CK])
            dr1 = area.new(f"dr1{layer}", [8, CK])
            dsp = area.new(f"dsp{layer}", [8, 3, CK], BF)

        t_c = None
        for b_ in Qs + Ks:
            t_c = pool.put(lambda e, b_=b_: e.memset(b_[96:K2, :, :], 1.0))
        for b_ in Va:
            t_c = pool.put(lambda e, b_=b_: e.memset(b_[:, :, :, :], 1.0))
        S_ = {"free_sp": [(), ()]}
        sfree = {"tq": None, "rq": None, "z": (), "zT": ()}
        q_ready, k_ready, v_ready = {}, {}, {}
        chunk_done = {}

        def split(src, src_waits, evac, n):
            i, b3, free = SP3.take()
            t0 = evac(tq, [*src_waits, sfree["tq"]])
            ta = pool.put(lambda e: e.tensor_copy(b3[:, 0, 0:n], tq[:, 0:n]), [t0, *free])
            tb = pool.put(lambda e: e.tensor_tensor(rq[:, 0:n], tq[:, 0:n], b3[:, 0, 0:n], ALU.subtract),
                          [ta, sfree["rq"]])
            tc = dve.put(lambda e: e.tensor_copy(b3[:, 1, 0:n], rq[:, 0:n]), [tb, *free])
            td = dve.put(lambda e: e.tensor_tensor(b3[:, 2, 0:n], rq[:, 0:n], b3[:, 1, 0:n], ALU.subtract), [tc])
            sfree["tq"], sfree["rq"] = tb, td
            return i, b3, (ta, td), t0

        def stack(dst, col, n, half, b3, parts, waits):
            return dq.group(sp, [
                lambda e, i=i, p=p: e.dma_start(dst[16 * i:16 * i + 16, 8 * half:8 * half + 8, col:col + n],
                                                b3[:, p, 0:n])
                for i, p in enumerate(parts)], waits)

        def context():
            t = dw.group(sp, [lambda e: e.dma_start(dr[:, :], D["delta"])])
            t = dve.put(lambda e: e.tensor_copy(dsp[:, 0, :], dr[:, :]), [t])
            t = dve.put(lambda e: e.tensor_tensor(dr1[:, :], dr[:, :], dsp[:, 0, :], ALU.subtract), [t])
            t = dve.put(lambda e: e.tensor_copy(dsp[:, 1, :], dr1[:, :]), [t])
            t = dve.put(lambda e: e.tensor_tensor(dsp[:, 2, :], dr1[:, :], dsp[:, 1, :], ALU.subtract), [t])
            kd = Ks[0][:, :, :].rearrange("p h (b s) -> p h b s", b=NB)
            tk = [dq.group(sp, [lambda e, i=i, h=h: e.dma_start(kd[96 + i:97 + i, h, :, :], dsp[:, i, :])
                                for i in range(3) for h in range(16)], [t, t_c])]
            for cc in range(2):
                for half in range(2):
                    i, bank, free = M.take()
                    for k in range(2):
                        tp = pe.put(lambda e, k=k, cc=cc, half=half, bank=bank: e.matmul(
                            bank[:, 0:480], wk[:, k, 128 * half:128 * half + 128], ctx[:, k, 480 * cc:480 * cc + 480],
                            start=k == 0, stop=k == 1), [t_W, t_ctx, *free])

                    def evac(d, w, bank=bank, half=half):
                        return act.put(lambda e: e.activation(d[:, 0:480], bank[:, 0:480], ACT.Identity,
                                                              bias=vcol(V_BK[layer] + half)), [*w, t_vec])
                    j, b3, ts, t0 = split(bank, [tp], evac, 480)
                    M.free[i] = (t0,)
                    g = stack(Ks[0], 480 * cc, 480, half, b3, KP, ts)
                    SP3.free[j] = (g,)
                    tk.append(g)
                    yield
            for b in range(NB):
                k_ready[b] = tk
                i, bank, free = M.take()
                for k in range(2):
                    tp = pe.put(lambda e, k=k, b=b, bank=bank: e.matmul(
                        bank[0:CK, 0:256], ctx[:, k, CK * b:CK * b + CK], wv[:, k, :], start=k == 0, stop=k == 1),
                        [t_W, t_ctx, *free])
                v_ready[b] = dve.put(lambda e, b=b, bank=bank: e.tensor_tensor(
                    Va[0][0:CK, b, :, 0:32:2], bank[0:CK, 0:256].rearrange("p (h r) -> p h r", r=16),
                    bv[0:CK, :].rearrange("p (h r) -> p h r", r=16), ALU.add), [tp, t_c])
                M.free[i] = (v_ready[b],)
                if b % 2:
                    yield

        def proj(c):
            tiles = range(4 * c, 4 * c + 4)
            slot = c % 3
            if layer == 1:
                t = norm([x[:, t, :] for t in tiles], [y[:, t, :] for t in tiles], [x_ready[t] for t in tiles])
                y_norm = t
                src = [y[:, t, :] for t in tiles]
                yield
            else:
                src, t = [x[:, t, :] for t in tiles], None
            t = norm(src, [z[:, i, :] for i in range(4)], [t, *(x_ready[t_] for t_ in tiles)], sfree["z"])
            dst = x if layer != 1 else y
            for i, tt in enumerate(tiles):
                r = pool.put(lambda e, tt=tt: e.tensor_tensor(dst[:, tt, :], dst[:, tt, :], bo, ALU.add), [t, t_W])
                x_ready[tt] = r
            tz = []
            rd = []
            yield
            for g in range(2):
                i, bank, free = M.take()
                for tt in range(2):
                    for k in range(2):
                        tp = pe.put(lambda e, g=g, tt=tt, k=k, bank=bank: e.transpose(
                            bank[:, 256 * k + 128 * tt:256 * k + 128 * tt + 128],
                            z[:, 2 * g + tt, 128 * k:128 * k + 128], idf[:, :]), [t, t_idf, *free])
                if layer == 1:
                    for k in range(2):
                        ta = act.put(lambda e, g=g, k=k, bank=bank: e.activation(
                            zT[:, k, 256 * g:256 * g + 256], bank[:, 256 * k:256 * k + 256], ACT.Identity,
                            bias=vcol(V_B1 + k), scale=vcol(V_G1 + k)), [tp, t_vec, *sfree["zT"]])
                else:
                    ta = act.put(lambda e, g=g, bank=bank: e.activation(
                        zT[:, :, 256 * g:256 * g + 256], bank[:, :].rearrange("p (k n) -> p k n", k=2), ACT.Identity),
                        [tp, *sfree["zT"]])
                M.free[i] = (ta,)
                tz.append(ta)
                rd.append(tp)
                yield
            sfree["z"] = tuple(rd)
            reads = []
            ends = chunk_done.get(c - 3, ())
            qr, kr = [], []
            for half in range(2):
                for what, w, vb in (("q", wq, V_BQ), ("k", wk, V_BK)):
                    if cross and what == "k":
                        continue
                    i, bank, free = M.take()
                    for k in range(2):
                        tp = pe.put(lambda e, k=k, half=half, bank=bank, w=w: e.matmul(
                            bank[:, :], w[:, k, 128 * half:128 * half + 128], zT[:, k, :], start=k == 0, stop=k == 1),
                            [t_W, *tz, *free])
                    reads.append(tp)

                    def evac(d, wts, bank=bank, half=half, what=what, vb=vb):
                        if what == "q" and cross:
                            for j in range(2):
                                b = 2 * c + j
                                r = act.put(lambda e, j=j, b=b: e.activation(
                                    d[:, 256 * j:256 * j + 256], bank[:, 256 * j:256 * j + 256], ACT.Identity,
                                    bias=tb[:, half, b:b + 1], scale=vcol(V_TAU + b)), [*wts, t_tb])
                            return r
                        return act.put(lambda e: e.activation(d[:, :], bank[:, :], ACT.Identity,
                                                              bias=vcol(vb[layer] + half)), [*wts, t_vec])
                    j, b3, ts, t0 = split(bank, [tp], evac, 512)
                    M.free[i] = (t0,)
                    d, parts, l = (Qs[slot], QP, qr) if what == "q" else (Ks[slot], KP, kr)
                    g = stack(d, 0, 512, half, b3, parts, [*ts, t_c, *ends])
                    SP3.free[j] = (g,)
                    l.append(g)
                    yield
            for b in (2 * c, 2 * c + 1):
                q_ready[b] = qr
                if not cross:
                    k_ready[b] = kr
            if not cross:
                for tt in range(4):
                    i, bank, free = M.take()
                    for k in range(2):
                        tp = pe.put(lambda e, k=k, tt=tt, bank=bank: e.matmul(
                            bank[:, 0:256], zT[:, k, 128 * tt:128 * tt + 128], wv[:, k, :], start=k == 0, stop=k == 1),
                            [t_W, *tz, *free])
                    reads.append(tp)
                    tv = dve.put(lambda e, tt=tt, bank=bank: e.tensor_tensor(
                        Va[slot][:, tt, :, 0:32:2], bank[:, 0:256].rearrange("p (h r) -> p h r", r=16),
                        bv.rearrange("p (h r) -> p h r", r=16), ALU.add), [tp, t_c, *ends])
                    M.free[i] = (tv,)
                    v_ready[2 * c + tt // 2] = tv
                    yield
            sfree["zT"] = tuple(reads)

        if cross:
            tb = area.new(f"tb{layer}", [128, 2, 8])
            for half in range(2):
                t_tb = pool.put(lambda e, half=half: e.tensor_scalar(
                    tb[:, half, :], vec[:, V_TAU:V_TAU + 8], vcol(V_BQ[layer] + half), None, ALU.mult), [t_vec])
        else:
            t_tb = None

        def qcol(b, n=256, o=0):
            return (b // 2) % 3, 256 * (b % 2) + o, n

        def keys(b, h, kt, rows):
            if cross:
                return Ks[0][0:rows, h, CK * b:CK * b + CK]
            s, c0, _ = qcol(b)
            return Ks[s][0:rows, h, c0 + 128 * kt:c0 + 128 * kt + 128]

        m_ready = {}
        nm_t = {}
        HU = 4 if cross else 2

        def maxima(b):
            s, c0, _ = qcol(b)
            gm, mt, mfree = mT.take()
            ths = []
            for qt in range(2):
                last = None
                for u in range(16 // HU):
                    i, bank, free = M.take()
                    for j in range(HU):
                        h = u * HU + j
                        if cross:
                            tp = pe.put(lambda e, h=h, j=j, bank=bank, qt=qt: e.matmul(
                                bank[:, CK * j:CK * j + CK], Qs[s][0:K1, h, c0 + 128 * qt:c0 + 128 * qt + 128],
                                keys(b, h, 0, K1), start=True, stop=True), [*q_ready[b], *k_ready[b], *free])
                        else:
                            tp = pe.put(lambda e, h=h, j=j, bank=bank, qt=qt: e.matmul(
                                bank[:, 256 * j:256 * j + 256], Qs[s][0:K1, h, c0 + 128 * qt:c0 + 128 * qt + 128],
                                Ks[s][0:K1, h, c0:c0 + 256], start=True, stop=True),
                                [*q_ready[b], *k_ready[b], *free])
                    last = dve.put(lambda e, u=u, bank=bank: e.tensor_reduce(
                        nm[:, u * HU:u * HU + HU],
                        bank[:, 0:480].rearrange("p (h s) -> p h s", h=4) if cross else
                        bank[:, :].rearrange("p (h s) -> p h s", h=2),
                        AX.X, ALU.max, negate=True), [tp, nm_t.get("free")])
                    M.free[i] = (last,)
                    yield
                k, mh, hfree = Mh.take()
                ta = pool.put(lambda e, mh=mh: e.tensor_copy(mh[:, 0:16], nm[:, :]), [last, *hfree])
                tb_ = pool.put(lambda e, mh=mh: e.tensor_tensor(mh[:, 16:32], nm[:, :], mh[:, 0:16], ALU.subtract), [ta])
                nm_t["free"] = tb_
                ths.append((k, mh, tb_))
            yield
            i, bank, free = M.take()
            for qt, (k, mh, t) in enumerate(ths):
                tp = pe.put(lambda e, mh=mh, bank=bank, qt=qt: e.matmul(
                    bank[0:32, 128 * qt:128 * qt + 128], mh[:, :], idb[:, :], start=True, stop=True),
                    [t, t_idb, *free])
                Mh.free[k] = (tp,)
            tc = act.put(lambda e, bank=bank: e.activation(mt[:, :], bank[0:32, 0:256], ACT.Identity), [tp, *mfree])
            M.free[i] = (tc,)
            g = dm.group(sp, [lambda e: e.dma_start(Qs[s][K1:K2, :, c0:c0 + 256], mt[:, :])], [tc, t_c])
            mT.free[gm] = (g,)
            m_ready[b] = g

        def heads(b):
            s, c0, _ = qcol(b)
            UN = 4 if cross else 8
            pend = []
            ol_i, ol, ol_free = OL.take()
            og = []

            def values(u, p_i, p, t_e):
                if cross:
                    hg, js = u, range(4)
                else:
                    hg, js = u // 2, (2 * (u % 2), 2 * (u % 2) + 1)
                half, gg = hg // 2, hg % 2
                for n, j in enumerate(js):
                    h = 8 * half + 4 * gg + j
                    for kt in range(KT):
                        v = Va[0][0:CK, b, h, :] if cross else Va[s][:, 2 * (b % 2) + kt, h, :]
                        src = p[0:NK, 256 * n:256 * n + 256] if cross else p[:, 512 * n + 256 * kt:512 * n + 256 * kt + 256]
                        tp = pe.put(lambda e, j=j, v=v, src=src, kt=kt, gg=gg: e.matmul(
                            U[32 * j:32 * j + 32, 256 * gg:256 * gg + 256], v, src, start=kt == 0, stop=kt == KT - 1),
                            [t_e, v_ready[b], *ufree[0]])
                P.free[p_i] = (tp,)
                if gg == 1 and js[-1] == 3:
                    ui, ub, uf = Ub.take()
                    tu = act.put(lambda e: e.activation(ub[:, :], U[:, :], ACT.Identity), [tp, *uf])
                    ufree[0] = (tu,)
                    g = do.group(sp, [
                        lambda e, half=half, k=k: e.dma_start(ol[:, half, k, :], ub[k:128:2, :].rearrange("p (g q) -> p g q", g=2))
                        for k in range(2)], [tu, *ol_free])
                    Ub.free[ui] = (g,)
                    og.append(g)
                return tp

            for u in range(UN):
                si, ps, sfr = S.take()
                pi, p, pfr = P.take()
                for n in range(4):
                    if cross:
                        h, kt = 8 * (u // 2) + 4 * (u % 2) + n, 0
                    else:
                        hg = u // 2
                        h, kt = 8 * (hg // 2) + 4 * (hg % 2) + 2 * (u % 2) + n // 2, n % 2
                    tp = pe.put(lambda e, n=n, h=h, kt=kt, ps=ps: e.matmul(
                        ps[0:NK, 256 * n:256 * n + 256], keys(b, h, kt, K2), Qs[s][0:K2, h, c0:c0 + 256],
                        start=True, stop=True), [m_ready[b], *q_ready[b], *k_ready[b], *sfr])
                te = act.put(lambda e, ps=ps, p=p: e.activation(p[0:NK, :], ps[0:NK, :], ACT.Exp, scale=0.25),
                             [tp, *pfr])
                S.free[si] = (te,)
                pend.append((u, pi, p, te))
                yield
                if len(pend) > 1:
                    tl = values(*pend.pop(0))
            tl = values(*pend.pop(0))
            if b % 2:
                chunk_done[b // 2] = (tl,)
            outs[b] = (ol_i, ol, og)

        outs = {}
        dst = x if layer != 1 else y

        def project(b):
            ol_i, ol, og = outs.pop(b)
            t = dve.put(lambda e: e.reciprocal(ol[:, :, 1, :], ol[:, :, 1, :]), og)
            t = pool.put(lambda e: e.tensor_tensor(ol[:, :, 0, :], ol[:, :, 0, :], ol[:, :, 1, :], ALU.mult), [t])
            yield
            i, bank, free = M.take()
            for tt in range(2):
                for half in range(2):
                    tp = pe.put(lambda e, tt=tt, half=half, bank=bank: e.matmul(
                        bank[:, 256 * tt:256 * tt + 256], ol[:, half, 0, 128 * tt:128 * tt + 128], wo[:, half, :],
                        start=half == 0, stop=half == 1), [t, *free])
            t2 = dve.put(lambda e, bank=bank: e.tensor_tensor(
                dst[:, 2 * b:2 * b + 2, :], dst[:, 2 * b:2 * b + 2, :], bank[:, :].rearrange("p (t d) -> p t d", t=2),
                ALU.add), [tp, x_ready[2 * b], x_ready[2 * b + 1]])
            M.free[i] = (t2,)
            OL.free[ol_i] = (tp, t)
            x_ready[2 * b] = x_ready[2 * b + 1] = t2

        def step(g):
            if g is not None:
                try:
                    next(g)
                    return g
                except StopIteration:
                    return None

        def drain(g):
            while g is not None:
                g = step(g)

        def chain(*gs):
            for g in gs:
                yield from g

        if cross:
            drain(context())
        drain(proj(0))
        drain(proj(1))
        drain(maxima(0))
        drain(maxima(1))
        per = 2 if cross else 2
        side = None
        for b in range(NB):
            c = b // 2 + 2
            if b % 2 == 0 and c < 4:
                drain(side)
                side = proj(c)
            mx = maxima(b + 2) if b + 2 < NB else None
            if b % 2 == 1 and b + 1 < NB:
                pass
            if mx is not None and (b + 2) % 2 == 0:
                drain(side)
                side = None
            hd = heads(b)
            pj = project(b - 1) if b else None
            k = 0
            while hd is not None:
                hd = step(hd)
                for _ in range(3 if cross else 2):
                    mx = step(mx)
                side = step(side)
                if k == 2:
                    drain(pj)
                    pj = None
                k += 1
            drain(mx)
            drain(pj)
        drain(project(NB - 1))

    vals = {}

    def load(q, key, ap, waits, top):
        q.put(lambda e: vals.__setitem__(key, e.value_load(ap, min_val=0, max_val=top)), waits, signal=False)

    def moe_by_token(area):
        w1 = area.new("mw1", [128, 8, 2, 1024])
        w2 = area.new("mw2", [128, 8, 8, 256])
        b2 = area.new("mb2", [128, 8, 256])
        gw = area.new("gw", [128, 2, 8])
        t_gw = dw.group(sp, [lambda e: e.dma_start(gw[:, :, :], D["gw"])])
        t_b2 = dw.group(sp, [lambda e: e.dma_start(b2[:, :, :], D["b2"])])
        t_w1 = dw.group(act, [lambda e, k=k: e.dma_start(w1[:, k, :, :], D["mw1"][k]) for k in range(8)])
        t_w2 = dw.group(act, [lambda e, k=k: e.dma_start(w2[:, k, :, :], D["mw2"][k]) for k in range(8)])
        hT = Ring([area.new(f"ghT{i}", [128, 2, 256]) for i in range(2)])
        lg = area.new("lg", [128, NT, 8])
        mx = area.new("mx", [128, NT])
        ohb = area.new("ohb", [128, NT + 1, 8], BF)
        ltb = area.new("ltb", [128, 128], BF)
        oneb = area.new("oneb", [128, 128], BF)
        cmp_ = area.new("cmp", [128, 8, 16])
        nt = area.new("nt", [128, 8])
        tri = area.new("tri", [128, 8, 8])
        binc = area.new("binc", [128, 8])
        rk = area.new("rk", [128, NT, 8])
        posf = area.new("posf", [128, NT])
        pos = area.new("pos", [128, NT], I32)
        tej = area.new("tej", [128, NTILE, 8])
        tef = area.new("tef", [128, NTILE])
        te = area.new("te", [128, NTILE], I32)
        zt = Ring([area.new(f"zt{i}", [128, 256]) for i in range(3)])
        zT = Ring([area.new(f"mzT{i}", [128, 2, 128]) for i in range(2)])
        mid = Ring([area.new(f"mid{i}", [128, 1024]) for i in range(2)])
        mdT = Ring([area.new(f"mdT{i}", [128, 8, 128]) for i in range(2)])
        yt = Ring([area.new(f"yt{i}", [128, 256]) for i in range(3)])

        t_lt = pool.put(lambda e: e.tensor_copy(ltb[:, :], cst[:, C_LT:C_LT + 128]), [t_cst])
        t_lt = pool.put(lambda e: e.memset(oneb[:, :], 1.0))
        t_lt = pool.put(lambda e: e.memset(ohb[:, NT, :], 0.0))

        for c in range(4):
            tiles = range(4 * c, 4 * c + 4)
            ys = [y[:, t, :] for t in tiles]
            r = pool.put(lambda e, c=c: e.tensor_tensor(x[:, 4 * c:4 * c + 4, :], x[:, 4 * c:4 * c + 4, :],
                                                        y[:, 4 * c:4 * c + 4, :], ALU.add),
                         [x_ready[t] for t in tiles])
            t = norm(ys, ys, [r])
            for t_ in tiles:
                x_ready[t_] = t
            for g in range(2):
                i, bank, free = M.take()
                hi, h, hfree = hT.take()
                for tt in range(2):
                    for k in range(2):
                        tp = pe.put(lambda e, c=c, g=g, tt=tt, k=k, bank=bank: e.transpose(
                            bank[:, 256 * k + 128 * tt:256 * k + 128 * tt + 128],
                            y[:, 4 * c + 2 * g + tt, 128 * k:128 * k + 128], idf[:, :]), [t, *free])
                for k in range(2):
                    ta = act.put(lambda e, k=k, bank=bank, h=h: e.activation(
                        h[:, k, :], bank[:, 256 * k:256 * k + 256], ACT.Identity,
                        bias=vcol(V_B2 + k), scale=vcol(V_G2 + k)), [tp, *hfree])
                M.free[i] = (ta,)
                for tt in range(2):
                    n = 4 * c + 2 * g + tt
                    for k in range(2):
                        tl = pe.put(lambda e, n=n, tt=tt, k=k, h=h: e.matmul(
                            U[:, 8 * n:8 * n + 8], h[:, k, 128 * tt:128 * tt + 128], gw[:, k, :],
                            start=k == 0, stop=k == 1), [ta, t_gw, *ufree[0]])
                hT.free[hi] = (tl,)

        def v(fn, *w):
            return dve.put(fn, w)

        def over(ap, n, d):
            return ap.unsqueeze(d).broadcast_to([*ap.shape[:d], n, *ap.shape[d:]])

        gb = vec[:, V_GB:V_GB + 8]
        t = v(lambda e: e.tensor_tensor(lg[:, :, :], U[:, 0:128].rearrange("p (t e) -> p t e", e=8),
                                        over(gb, NT, 1), ALU.add), tl)
        ufree[0] = (t,)
        t = v(lambda e: e.tensor_reduce(mx[:, :], lg[:, :, :], AX.X, ALU.max), t)
        t = v(lambda e: e.tensor_tensor(lg[:, :, :], lg[:, :, :], over(mx[:, :], 8, 2), ALU.is_equal), t)
        t = v(lambda e: e.tensor_tensor(lg[:, :, :], lg[:, :, :], over(cst[:, C_DESC:C_DESC + 8], NT, 1), ALU.mult), t, t_cst)
        t = v(lambda e: e.tensor_reduce(mx[:, :], lg[:, :, :], AX.X, ALU.max), t)
        t = v(lambda e: e.tensor_tensor(oh[:, :, :], lg[:, :, :], over(mx[:, :], 8, 2), ALU.is_equal), t)
        t_oh = v(lambda e: e.tensor_copy(ohb[:, 0:NT, :], oh[:, :, :]), t)
        i, bank, free = M.take()
        tp = pe.put(lambda e: e.matmul(bank[:, 0:136], ltb[:, :], ohb[:, :, :], start=True, stop=False),
                    [t_oh, t_lt, *free])
        for s in range(NT):
            tp = pe.put(lambda e, s=s: e.matmul(bank[:, 8 * s + 8:136], oneb[:, :], over(ohb[:, s, :], NT - s, 1),
                                                start=False, stop=s == NT - 1))
        t = v(lambda e: e.tensor_tensor(cmp_[:, :, :], over(bank[:, 128:136], 16, 2),
                                        over(cst[:, C_K128:C_K128 + 16], 8, 1), ALU.is_gt), tp)
        t = v(lambda e: e.tensor_reduce(nt[:, :], cmp_[:, :, :], AX.X, ALU.add), t)
        t = v(lambda e: e.tensor_tensor(tri[:, :, :], over(nt[:, :], 8, 1),
                                        cst[:, C_TRI:C_TRI + 64].rearrange("p (a b) -> p a b", a=8), ALU.mult), t)
        t_b = v(lambda e: e.tensor_reduce(binc[:, :], tri[:, :, :], AX.X, ALU.add), t)
        t = v(lambda e: e.tensor_tensor(nt[:, :], binc[:, :], nt[:, :], ALU.subtract), t_b)
        t = v(lambda e: e.tensor_scalar(nt[:, :], nt[:, :], 128.0, None, ALU.mult), t)
        t = v(lambda e: e.tensor_tensor(rk[:, :, :], bank[:, 0:128].rearrange("p (t e) -> p t e", e=8),
                                        over(nt[:, :], NT, 1), ALU.add), t)
        M.free[i] = (t,)
        t = v(lambda e: e.tensor_tensor(rk[:, :, :], rk[:, :, :], oh[:, :, :], ALU.mult), t)
        t = v(lambda e: e.tensor_reduce(posf[:, :], rk[:, :, :], AX.X, ALU.add), t)
        t_pos = v(lambda e: e.tensor_copy(pos[:, :], posf[:, :]), t)
        t = v(lambda e: e.tensor_tensor(tej[:, :, :], over(binc[:, :], NTILE, 1),
                                        over(cst[:, C_J:C_J + NTILE], 8, 2), ALU.is_le), t_b)
        t = v(lambda e: e.tensor_reduce(tef[:, :], tej[:, :, :], AX.X, ALU.add), t)
        t = v(lambda e: e.tensor_scalar(tef[:, :], tef[:, :], 7.0, None, ALU.min), t)
        t_te = v(lambda e: e.tensor_copy(te[:, :], tef[:, :]), t)

        def slots(t_):
            return bass.IndirectOffsetOnAxis(ap=pos[:, t_:t_ + 1].bitcast(U32), axis=0)

        t_sc = ds.group(pool, [lambda e, n=n: e.indirect_dma_start(zb, slots(n), y[:, n, :], None)
                               for n in range(NT)], [t_pos, t_zero, *(x_ready[n] for n in range(NT))])

        zin, up_, ups = {}, {}, {}

        def fetch(j):
            i, b, free = zt.take()
            g = dz.group(sp, [lambda e: e.dma_start(b[:, :], zb[128 * j:128 * j + 128, :])], [t_sc, *free])
            zin[j] = (i, b, g)

        def front(j):
            i, b, g = zin.pop(j)
            bi, bank, free = M.take()
            for k in range(2):
                tp = pe.put(lambda e, k=k: e.transpose(bank[:, 128 * k:128 * k + 128], b[:, 128 * k:128 * k + 128],
                                                       idf[:, :]), [g, *free])
            zt.free[i] = (tp,)
            if j + 3 < NTILE:
                fetch(j + 3)
            zi, zz, zfree = zT.take()
            for k in range(2):
                ta = act.put(lambda e, k=k: e.activation(zz[:, k, :], bank[:, 128 * k:128 * k + 128], ACT.Identity,
                                                         bias=vcol(V_B2 + k), scale=vcol(V_G2 + k)), [tp, *zfree])
            M.free[bi] = (ta,)
            load(pe, ("e", j), te[0:1, j:j + 1], [t_te], 7)
            si, ps, sfr = S.take()
            for f in range(2):
                for k in range(2):
                    tp = pe.put(lambda e, f=f, k=k: e.matmul(
                        ps[:, 512 * f:512 * f + 512], zz[:, k, :],
                        w1[:, bass.ds(vals["e", j], 1), k, 512 * f:512 * f + 512], start=k == 0, stop=k == 1),
                        [ta, t_w1, *sfr])
            zT.free[zi] = (tp,)
            mi, m, mfr = mid.take()
            ta = act.put(lambda e: e.activation(m[:, 0:512], ps[:, 0:512], ACT.Identity), [tp, *mfr])
            tb = dve.put(lambda e: e.tensor_copy(m[:, 512:1024], ps[:, 512:1024]), [tp, *mfr])
            S.free[si] = (ta, tb)
            ups[j] = (mi, m, ta, tb)

        def back(j):
            mi, m, ta, tb = ups.pop(j)
            di, md, dfr = mdT.take()
            load(act, ("a", j), te[0:1, j:j + 1], [t_te], 7)
            load(dve, ("d", j), te[0:1, j:j + 1], [t_te], 7)
            outs = []
            for g in range(2):
                bi, bank, free = M.take()
                for k in range(4):
                    tp = pe.put(lambda e, g=g, k=k, bank=bank: e.transpose(
                        bank[:, 128 * k:128 * k + 128], m[:, 512 * g + 128 * k:512 * g + 128 * k + 128], idf[:, :]),
                        [ta if g == 0 else tb, *free])
                for k in range(4):
                    f = 4 * g + k
                    if g == 0:
                        to = act.put(lambda e, f=f, k=k, bank=bank: e.activation(
                            md[:, f, :], bank[:, 128 * k:128 * k + 128], ACT.Relu,
                            bias=vec[:, bass.ds(vals["a", j] * 8 + (V_BF1 + f), 1)]), [tp, *dfr])
                    else:
                        to = dve.put(lambda e, f=f, k=k, bank=bank: e.tensor_scalar(
                            md[:, f, :], bank[:, 128 * k:128 * k + 128],
                            vec[:, bass.ds(vals["d", j] * 8 + (V_BF1 + f), 1)], 0.0, ALU.add, ALU.max), [tp, *dfr])
                M.free[bi] = (to,)
                outs.append(to)
            mid.free[mi] = (tp,)
            for f in range(8):
                tp = pe.put(lambda e, f=f: e.matmul(U[:, 0:256], md[:, f, :], w2[:, bass.ds(vals["e", j], 1), f, :],
                                                    start=f == 0, stop=f == 7), [*outs, t_w2, *ufree[0]])
            mdT.free[di] = (tp,)
            yi, yo, yfr = yt.take()
            t = dve.put(lambda e: e.tensor_tensor(yo[:, :], U[:, 0:256], b2[:, bass.ds(vals["d", j], 1), :], ALU.add),
                        [tp, t_b2, *yfr])
            ufree[0] = (t,)
            g = dy.group(sp, [lambda e: e.dma_start(yb[128 * j:128 * j + 128, :], yo[:, :])], [t])
            yt.free[yi] = (g,)
            ydone[j] = g

        ydone = {}
        for j in range(3):
            fetch(j)
        front(0)
        for j in range(NTILE):
            if j + 1 < NTILE:
                front(j + 1)
            back(j)
        gat = [dg.group(pool, [lambda e, n=n: e.indirect_dma_start(y[:, n, :], None, yb, slots(n))],
                        [t_sc, *ydone.values()]) for n in range(NT)]
        for n in range(NT):
            x_ready[n] = dve.put(lambda e, n=n: e.tensor_tensor(x[:, n, :], x[:, n, :], y[:, n, :], ALU.add), [gat[n]])

    def moe_by_expert(area):
        wc = area.new("wc", [128, 2, 128])
        t_wc = dw.group(sp, [lambda e: e.dma_start(wc[:, :, :], D["wc"])])
        v1 = area.new("v1", [128, 2, 128, 32])
        t_v1 = dw.group(sp, [lambda e: e.dma_start(v1[:, :, :, :], D["v1"])])
        v2 = area.new("v2", [128, 32, 256])
        t_v2 = dw.group(sp, [lambda e: e.dma_start(v2[:, :, :], D["v2"])])
        c2 = area.new("c2", [128, 256])
        t_c2 = dw.group(sp, [lambda e: e.dma_start(c2[:, :], D["c2"])])
        zT = area.new("ezT", [128, 2, 512])
        perm = area.new("perm", [128, 64, 32])
        gmx = area.new("gmx", [128, 16])
        pT = Ring([area.new(f"pT{i}", [128, 4, 128], BF) for i in range(1)])
        z3 = Ring([area.new(f"z3{i}", [128, 3, 4, 256], BF) for i in range(1)])
        rz = area.new("rz", [128, 4, 256])
        G = area.new("G", [128, 2, 128, 64])
        tmp = area.new("etmp", [128, 8, 64])
        BD = Ring([area.new(f"BD{i}", [128, 8, 4, 64]) for i in range(2)])
        for b_ in BD.bufs:
            t_bd = pool.put(lambda e, b_=b_: e.memset(b_[:, :, :, :], 0.0))

        def over(ap, n, d):
            return ap.unsqueeze(d).broadcast_to([*ap.shape[:d], n, *ap.shape[d:]])

        t_rd = None
        zT_free = None
        rz_free = None
        perm_t, G_t = {}, []
        for c in range(4):
            tiles = range(4 * c, 4 * c + 4)
            t = norm([x[:, t, :] for t in tiles], [y[:, t, :] for t in tiles], [x_ready[t] for t in tiles])
            zi, z, zfr = z3.take()
            yc = y[:, 4 * c:4 * c + 4, :]
            ta = pool.put(lambda e, z=z, yc=yc: e.tensor_copy(z[:, 0, :, :], yc), [t, *zfr])
            tb = pool.put(lambda e, z=z, yc=yc: e.tensor_tensor(rz[:, :, :], yc, z[:, 0, :, :], ALU.subtract), [ta, rz_free])
            tc = dve.put(lambda e, z=z: e.tensor_copy(z[:, 1, :, :], rz[:, :, :]), [tb, *zfr])
            td = dve.put(lambda e, z=z: e.tensor_tensor(z[:, 2, :, :], rz[:, :, :], z[:, 1, :, :], ALU.subtract), [tc])
            rz_free = td
            for g in range(2):
                i, bank, free = M.take()
                for tt in range(2):
                    for k in range(2):
                        tp = pe.put(lambda e, c=c, g=g, tt=tt, k=k, bank=bank: e.transpose(
                            bank[:, 256 * k + 128 * tt:256 * k + 128 * tt + 128],
                            y[:, 4 * c + 2 * g + tt, 128 * k:128 * k + 128], idf[:, :]), [t, *free])
                tz = act.put(lambda e, g=g, bank=bank: e.activation(
                    zT[:, :, 256 * g:256 * g + 256], bank[:, :].rearrange("p (k n) -> p k n", k=2), ACT.Identity),
                    [tp, zT_free])
                M.free[i] = (tz,)
            i, bank, free = M.take()
            for k in range(2):
                tp = pe.put(lambda e, k=k, bank=bank: e.matmul(bank[:, :], wc[:, k, :], zT[:, k, :],
                                                               start=k == 0, stop=k == 1), [tz, t_wc, *free])
            zT_free = tp
            pc = perm[:, 16 * c:16 * c + 16, :]
            t1 = act.put(lambda e, pc=pc, bank=bank: e.activation(
                pc, bank[:, :].rearrange("p (n t) -> p n t", t=32), ACT.Identity, bias=vcol(V_BC)), [tp])
            M.free[i] = (t1,)
            t1 = dve.put(lambda e, pc=pc: e.tensor_tensor(pc, pc, over(cst[:, C_TIE:C_TIE + 32], 16, 1), ALU.add), [t1, t_cst])
            t1 = dve.put(lambda e, pc=pc: e.tensor_reduce(gmx[:, :], pc, AX.X, ALU.max), [t1])
            t1 = dve.put(lambda e, pc=pc: e.tensor_tensor(pc, pc, over(gmx[:, :], 32, 2), ALU.is_equal), [t1])
            for t_ in tiles:
                perm_t[t_] = t1
            i, bank, free = M.take()
            for tt in range(4):
                tp = pe.put(lambda e, c=c, tt=tt, bank=bank: e.transpose(
                    bank[:, 128 * tt:128 * tt + 128], perm[:, 16 * c + 4 * tt:16 * c + 4 * tt + 4, :], idf[:, :]),
                    [t1, *free])
            pi, p_, pfr = pT.take()
            t2 = act.put(lambda e, p_=p_, bank=bank: e.activation(
                p_[:, :, :], bank[:, :].rearrange("p (t s) -> p t s", t=4), ACT.Identity), [tp, *pfr])
            M.free[i] = (t2,)
            for k in range(2):
                frees = [f for fr in S.free for f in fr]
                for tt in range(4):
                    for r in range(4):
                        for part in range(3):
                            o_ = PS[r // 2][:, 512 * (r % 2) + 128 * tt:512 * (r % 2) + 128 * tt + 128]
                            tp = pe.put(lambda e, o_=o_, r=r, part=part, tt=tt, k=k, z=z, p_=p_: e.matmul(
                                o_, z[32 * r:32 * r + 32, part, tt, 128 * k:128 * k + 128],
                                p_[32 * r:32 * r + 32, tt, :], start=part == 0, stop=part == 2),
                                [t2, td, *frees])
                for i in range(2):
                    gd = G[:, k, :, 16 * c:16 * c + 16].rearrange("p s (t r) -> p r t s", r=4)[:, 2 * i:2 * i + 2]
                    q = (act, dve)[i]
                    src = PS[i][:, :].rearrange("p (r t s) -> p r t s", r=2, t=4)
                    for r in range(2):
                        if i == 0:
                            tg = q.put(lambda e, gd=gd, src=src, r=r: e.activation(gd[:, r], src[:, r], ACT.Identity), [tp])
                        else:
                            tg = q.put(lambda e, gd=gd, src=src, r=r: e.tensor_copy(gd[:, r], src[:, r]), [tp])
                    S.free[i] = (tg,)
                    G_t.append(tg)
            pT.free[pi] = (tp,)
            z3.free[zi] = (tp,)
        Yn = Ring([rz[:, 0:2, :], rz[:, 2:4, :]])
        Yn.free = [(rz_free,), (rz_free,)]
        Yt = []
        up = {}

        tmp_free = [()]

        def first(b):
            i, bank, free = M.take()
            for q in range(8):
                for j in range(4):
                    s = 4 * (8 * b + q) + j
                    for k in range(2):
                        tp = pe.put(lambda e, q=q, j=j, s=s, k=k: e.matmul(
                            bank[32 * j:32 * j + 32, 64 * q:64 * q + 64], v1[:, k, s, :], G[:, k, s, :],
                            start=k == 0, stop=k == 1), [*G_t, t_v1, *free])
            t = dve.put(lambda e: e.tensor_tensor(tmp[:, :, :], bank[:, :].rearrange("p (q n) -> p q n", q=8),
                                                  over(vec[:, V_BM1 + 8 * b:V_BM1 + 8 * b + 8], 64, 2), ALU.add),
                        [tp, *tmp_free[0]])
            M.free[i] = (t,)
            bi, bd, bfr = BD.take()
            for j in range(4):
                ta = act.put(lambda e, j=j: e.activation(bd[32 * j:32 * j + 32, :, j, :], tmp[32 * j:32 * j + 32, :, :],
                                                         ACT.Relu), [t, t_bd, *bfr])
            tmp_free[0] = (ta,)
            up[b] = (bi, bd, ta)

        def second(b):
            bi, bd, ta = up.pop(b)
            for q in range(8):
                i, bank, free = M.take()
                for k in range(2):
                    tp = pe.put(lambda e, q=q, k=k, bank=bank: e.matmul(
                        bank[:, 256 * k:256 * k + 256], v2[:, 8 * b + q, 128 * k:128 * k + 128], bd[:, q, :, :],
                        start=True, stop=True), [ta, t_v2, *free])
                s = 4 * (8 * b + q)
                src = bank[:, :].rearrange("p (k s n) -> p k s n", k=2, s=4)
                if q % 2:
                    t = dve.put(lambda e, s=s, src=src: e.tensor_copy(G[:, :, s:s + 4, :], src), [tp])
                else:
                    t = act.put(lambda e, s=s, src=src: e.activation(G[:, :, s:s + 4, :], src, ACT.Identity), [tp])
                M.free[i] = (t,)
                Yt.append(t)
            BD.free[bi] = (tp,)

        first(0)
        for b in range(4):
            if b + 1 < 4:
                first(b + 1)
            second(b)
        ov = out.rearrange("(t p) d -> p t d", p=128)
        yn = {}

        def turn(m):
            i, bank, free = M.take()
            for n in range(2):
                for k in range(2):
                    tp = pe.put(lambda e, n=n, k=k: e.transpose(
                        bank[:, 256 * n + 128 * k:256 * n + 128 * k + 128], G[:, k, :, 2 * m + n], idf[:, :]),
                        [*Yt[-2:], *free])
            yi, yb_, yfr = Yn.take()
            t = dve.put(lambda e: e.tensor_tensor(yb_[:, :, :], bank[:, :].rearrange("p (n d) -> p n d", n=2),
                                                  over(c2[:, :], 2, 1), ALU.add), [tp, t_c2, *yfr])
            M.free[i] = (t,)
            yn[m] = (yi, yb_, t)

        state = {}

        def combine(m):
            yi, yb_, t = yn.pop(m)
            tile, half = m // 2, m % 2
            if half == 0:
                state["ps"] = S.take()
            si, ps, sfr = state["ps"]
            for n in range(2):
                j = 2 * half + n
                tp = pe.put(lambda e, n=n, j=j: e.matmul(ps[32 * j:32 * j + 32, 0:256], perm[:, 2 * m + n, :],
                                                         yb_[:, n, :], start=True, stop=True),
                            [t, perm_t[tile], *sfr])
            Yn.free[yi] = (tp,)
            if half:
                t = dve.put(lambda e: e.tensor_tensor(x[:, tile, :], x[:, tile, :], ps[:, 0:256], ALU.add), [tp])
                S.free[si] = (t,)
                if tile % 2:
                    dx.group(sp, [lambda e: e.dma_start(ov[:, tile - 1:tile + 1, :], x[:, tile - 1:tile + 1, :])], [t])

        turn(0)
        for m in range(32):
            if m + 1 < 32:
                turn(m + 1)
            combine(m)

    C_DESC, C_K128, C_LT, C_J, C_TIE, C_TRI = 0, 8, 24, 152, 175, 207
    cst = g0.new("cst", [128, 271])
    zero = g0.new("zero", [128, 256])
    nxt = g0.p
    t_cst = dw.group(sp, [lambda e: e.dma_start(cst[:, :], D["cst"])])
    t_z0 = pool.put(lambda e: e.memset(zero[:, :], 0.0))
    t_zero = dx.group(act, [lambda e, a=a: e.dma_start(zb[128 * a:128 * a + 128, :], zero[:, :])
                            for a in range(NTILE)], [t_z0])

    def all_done():
        ts = [(q.sem, q.n) for q in (pe, act, dve, pool) if q.n]
        for d in (dq, dm, do, dw, ds, dg, dz, dy, dx):
            ts += [(s, c) for s, c in zip(d.sems, d.count) if c]
        for q in (pe, act, dve, pool, sp):
            q.items.append((tuple(ts), None, None))

    attention(0, Area(nxt))
    if stage >= 2:
        all_done()
        attention(1, Area(nxt))
    if stage >= 3:
        all_done()
        moe_by_token(Area(nxt))
    if stage >= 4:
        all_done()
        attention(2, Area(nxt))
    if stage >= 5:
        all_done()
        moe_by_expert(Area(nxt))
    else:
        src = y if stage == 2 else x
        ov = out.rearrange("(t p) d -> p t d", p=128)
        dx.group(sp, [lambda e: e.dma_start(ov, src[:, :, :])], [x_ready[t] for t in range(NT)])
    for s, c in zip(dx.sems, dx.count):
        if c:
            sp.items.append((((s, c),), None, None))

    def run(q, eng):
        seen = {}
        for waits, fn, sm in q.items:
            for s, v in waits:
                if seen.get(s.name, 0) < v:
                    eng.wait_ge(s, v)
                    seen[s.name] = v
            if fn is None:
                continue
            ins = fn(eng)
            if isinstance(sm, tuple):
                ins.then_inc(sm[0], 16)
            elif sm is not None:
                ins.then_inc(sm, 1)

    with nc.Block() as block:
        block.tensor(lambda e: run(pe, e))
        block.scalar(lambda e: run(act, e))
        block.vector(lambda e: run(dve, e))
        block.gpsimd(lambda e: run(pool, e))
        block.sync(lambda e: run(sp, e))


STAGE = 5


def _layouts(i):
    import numpy as np
    f = np.float32
    A = {}
    A["x"] = np.ascontiguousarray(i["x"]).reshape(2048, 256)
    A["ctx"] = np.ascontiguousarray(
        i["ctx_1024"].reshape(960, 256).T.reshape(2, 128, 960).transpose(1, 0, 2))
    A["delta"] = np.ascontiguousarray(i["fside_BxS2_0"])
    A["idf"] = np.eye(128, dtype=f)

    def cols(w):
        return w.reshape(-1, 2, 8, 16).transpose(0, 1, 3, 2).reshape(-1, 256)

    def kin(w):
        return w.reshape(2, 128, -1).transpose(1, 0, 2).reshape(128, -1)

    def rows(w):
        return w.reshape(2, 2, 4, 16, 256).transpose(2, 3, 1, 0, 4).reshape(128, -1)

    def bc(v):
        return np.broadcast_to(v.reshape(1, -1), (128, v.size))

    def hv(v):
        return v.reshape(2, 8, 16).transpose(2, 1, 0).reshape(128, 2)

    def dv(v):
        return v.reshape(-1, 128).T

    sets = []
    for n in ("L0_xcond", "L0_ffn", "L1_xcond"):
        if n == "L0_ffn":
            sets.append((i[n + "_wq"], i[n + "_wk"], i[n + "_wv"], i[n + "_wo"],
                         i[n + "_bq"], i[n + "_bk"], i[n + "_bv"], i[n + "_bo"]))
        else:
            sets.append((i[n + "_Wq"].T, i[n + "_Wk"].T, i[n + "_Wv"].T, i[n + "_Wo"].T,
                         i[n + "_bq"], i[n + "_bk"], i[n + "_bv"], i[n + "_bo"]))
    vec = []
    for l, (q, k, v, o, bq, bk, bv, bo) in enumerate(sets):
        A[f"W{l}"] = np.ascontiguousarray(np.concatenate(
            [kin(cols(q)), kin(cols(k)), kin(v), rows(o), bc(bv), bc(bo)], axis=1))
        vec += [hv(bq), hv(bk)]
    vec += [dv(i["L0_ffn_ln1_g"]), dv(i["L0_ffn_ln1_b"]), dv(i["L0_ffn_ln2_g"]), dv(i["L0_ffn_ln2_b"]),
            bc(i["condB_tau"]), i["L1_ffn_bc"].reshape(128, 1),
            i["L1_ffn_b1"].reshape(32, 128).T, i["L0_ffn_b1"].reshape(64, 128).T, bc(i["L0_ffn_gate_b"])]
    A["gw"] = np.ascontiguousarray(kin(i["L0_ffn_gate_w"]).reshape(128, 2, 8))
    A["b2"] = np.ascontiguousarray(bc(i["L0_ffn_b2"].reshape(-1)).reshape(128, 8, 256))
    A["mw1"] = np.ascontiguousarray(i["L0_ffn_w1"].reshape(8, 2, 128, 1024).transpose(0, 2, 1, 3))
    A["mw2"] = np.ascontiguousarray(i["L0_ffn_w2"].reshape(8, 8, 128, 256).transpose(0, 2, 1, 3))
    A["wc"] = np.ascontiguousarray(i["L1_ffn_Wc"].reshape(2, 128, 128).transpose(1, 0, 2))
    A["v1"] = np.ascontiguousarray(i["L1_ffn_W1"].reshape(128, 2, 128, 32).transpose(2, 1, 0, 3))
    A["v2"] = np.ascontiguousarray(
        i["L1_ffn_W2"].reshape(32, 4, 256, 32).transpose(1, 3, 0, 2).reshape(128, 32, 256))
    A["c2"] = np.ascontiguousarray(i["L1_ffn_b2"].reshape(128, 256))
    k = np.arange
    A["cst"] = np.ascontiguousarray(np.concatenate([
        bc((8 - k(8)).astype(f)), bc((128 * k(16)).astype(f)), np.triu(np.ones((128, 128), f), 1),
        bc(k(NTILE).astype(f)), bc(np.linspace(0.0, 1e-6, 32, dtype=f)), bc(np.tril(np.ones((8, 8), f)))], axis=1))
    A["vec"] = np.ascontiguousarray(np.concatenate(vec, axis=1))
    return A


def kernel(**inputs):
    import numpy as np
    import concourse.bacc as bacc
    from concourse.bass_utils import run_bass_kernel_spmd as run
    i = {k: np.asarray(v) for k, v in inputs.items()}
    nc = bacc.Bacc("TRN2", target_bir_lowering=False, num_devices=1)
    A = _layouts(i)
    arrays = {f"in_{k}": v for k, v in A.items()}
    D = {k: nc.dram_tensor(f"in_{k}", v.shape, mybir.dt.from_np(v.dtype), kind="ExternalInput").ap()
         for k, v in A.items()}
    o = nc.dram_tensor("out_0", (2048, 256), F32, kind="ExternalOutput").ap()
    program(nc, D, o, STAGE)
    r = run(nc, [arrays], core_ids=[0])
    return r.results[0]["out_0"].reshape(8, 256, 256)
```
